# Optimizing a Trainium2 kernel written in Bass

```python
import numpy as np
import jax
import jax.numpy as jnp

def _softmax(x, axis=-1):
    return jax.nn.softmax(x, axis=axis)

def _gelu(x):
    return jax.nn.gelu(x, approximate=True)

def _silu(x):
    return jax.nn.silu(x)

def _sigmoid(x):
    return jax.nn.sigmoid(x)

def _layernorm(x, axis=-1, eps=1e-05):
    m = jnp.mean(x, axis=axis, keepdims=True)
    v = jnp.var(x, axis=axis, keepdims=True)
    return (x - m) / jnp.sqrt(v + eps)

def _scatter_add(tgt, idx, src, axis=0):
    return tgt.at[idx].add(src)

def _segment_sum(src, seg, n):
    return jax.ops.segment_sum(src, seg, n)
kernel_name = 'mk_adj_resnorm_d1_adj_r2_84cb25'

def setup_inputs(seed: int=0):
    np.random.seed(seed)
    _w = jnp.asarray

    def _rec_inputs():
        import jax
        import jax.numpy as jnp
        _gk = jax.random.key(seed)
        x = -0.000929 + 1 * jax.random.normal(jax.random.fold_in(_gk, 1), (8192, 128), jnp.float32)
        _a = jax.random.bernoulli(jax.random.fold_in(_gk, 2), 0.00195312, (8192, 8192))
        _af = _a.astype(jnp.float32)
        adj = _af
        return (x, adj)
    x, adj = _rec_inputs()

    def _L0_gnn_setup():
        import jax, jax.numpy as jnp
        import numpy as np
        N, D_IN, D_OUT, D_THETA = (4096, 128, 128, 128)
        BN_EPS = 1e-05
        NEG_FILL = jnp.float32(-9000000000000000.0)
        LEAKY_SLOPE = 0.01

        def _leaky_relu(x):
            return jnp.where(x > 0, x, LEAKY_SLOPE * x)
        key = jax.random.key(seed)
        ks = jax.random.split(key, 6)
        H = jax.random.normal(ks[0], (N, D_IN), jnp.float32)
        A = jax.random.randint(ks[1], (N, N), 0, 2).astype(jnp.float32)
        gamma = jnp.ones((D_IN,), jnp.float32)
        beta = jnp.zeros((D_IN,), jnp.float32)
        Wt = jax.random.normal(ks[2], (D_IN, D_THETA), jnp.float32) * 0.05
        bt = jnp.zeros((D_THETA,), jnp.float32)
        W1 = jax.random.normal(ks[3], (D_IN, D_OUT // 2), jnp.float32) * 0.05
        b1 = jnp.zeros((D_OUT // 2,), jnp.float32)
        W2 = jax.random.normal(ks[4], (D_IN, D_OUT // 2), jnp.float32) * 0.05
        b2 = jnp.zeros((D_OUT // 2,), jnp.float32)
        return {'H': H, 'A': A, 'gamma': gamma, 'beta': beta, 'Wt': Wt, 'bt': bt, 'W1': W1, 'b1': b1, 'W2': W2, 'b2': b2}
    _L0_gnn_all = _L0_gnn_setup()
    _L0_gnn_in = {k: v for k, v in _L0_gnn_all.items() if k in ('gamma', 'beta', 'Wt', 'bt', 'W1', 'b1', 'W2', 'b2')}
    del _L0_gnn_all
    return {'x': x, 'adj': adj, 'L0_gnn_gamma': _L0_gnn_in['gamma'], 'L0_gnn_beta': _L0_gnn_in['beta'], 'L0_gnn_Wt': _L0_gnn_in['Wt'], 'L0_gnn_bt': _L0_gnn_in['bt'], 'L0_gnn_W1': _L0_gnn_in['W1'], 'L0_gnn_b1': _L0_gnn_in['b1'], 'L0_gnn_W2': _L0_gnn_in['W2'], 'L0_gnn_b2': _L0_gnn_in['b2']}

def reference(x, adj, L0_gnn_gamma, L0_gnn_beta, L0_gnn_Wt, L0_gnn_bt, L0_gnn_W1, L0_gnn_b1, L0_gnn_W2, L0_gnn_b2):
    import jax
    import jax.numpy as jnp

    def _L0_gnn_ref(H, A, gamma, beta, Wt, bt, W1, b1, W2, b2):
        import jax, jax.numpy as jnp
        import numpy as np
        N, D_IN, D_OUT, D_THETA = (4096, 128, 128, 128)
        BN_EPS = 1e-05
        NEG_FILL = jnp.float32(-9000000000000000.0)
        LEAKY_SLOPE = 0.01

        def _leaky_relu(x):
            return jnp.where(x > 0, x, LEAKY_SLOPE * x)
        mean = jnp.mean(H, axis=0)
        var = jnp.var(H, axis=0)
        Hn = (H - mean) * jax.lax.rsqrt(var + BN_EPS) * gamma + beta
        Hx = Hn @ Wt + bt
        e = jax.nn.sigmoid(Hx @ Hx.T)
        mask = jnp.ceil(A * 0.01) > 0
        Am = jnp.where(mask, e, NEG_FILL)
        idx = jnp.arange(A.shape[0])
        Am = Am.at[idx, idx].set(1.0)
        Aw = jax.nn.softmax(Am, axis=1)
        out1 = _leaky_relu(Hn @ W1 + b1)
        out2 = _leaky_relu(Aw @ (Hn @ W2 + b2))
        return jnp.concatenate([out1, out2], axis=-1)
    x = _layernorm(x + _L0_gnn_ref(x, adj, L0_gnn_gamma, L0_gnn_beta, L0_gnn_Wt, L0_gnn_bt, L0_gnn_W1, L0_gnn_b1, L0_gnn_W2, L0_gnn_b2), axis=-1)
    return x

_drawn_inputs = setup_inputs


def setup_inputs(seed=0):
    import zlib

    import numpy as np

    out = dict(_drawn_inputs(seed))
    spreads = {'L0_gnn_gamma': (1.0, 0.2),
     'L0_gnn_beta': (0.0, 0.1),
     'L0_gnn_bt': (0.0, 0.8),
     'L0_gnn_b1': (0.0, 0.1),
     'L0_gnn_b2': (0.0, 0.1)}
    factors = {'L0_gnn_Wt': 3.229}
    for name, (base, spread) in spreads.items():
        noise = np.random.default_rng([zlib.crc32(name.encode()), seed]).standard_normal(out[name].shape)
        drawn = base * np.exp(spread * noise) if base else spread * noise
        out[name] = jnp.asarray(drawn.astype(out[name].dtype))
    for name, factor in factors.items():
        out[name] = (out[name] * factor).astype(out[name].dtype)
    return out
```

```python
import math
from contextlib import ExitStack

import concourse.bass as bass
from concourse import mybir

F32 = mybir.dt.float32
F16 = mybir.dt.float16
BF16 = mybir.dt.bfloat16
ALU = mybir.AluOpType
ACT = mybir.ActivationFunctionType
AX = mybir.AxisListType

BN_EPS = 1e-5
LN_EPS = 1e-5
LEAKY = 0.01
HS = 32.0
GS = 64.0
PS = 64.0

P = 128


def gnn_kernel(nc, x, adj, gamma, beta, Wt, bt, W1, b1, W2, b2, out):
    N, D = x.shape
    DH = W2.shape[1]
    NB = N // P
    GB = 4
    GW = GB * P
    NG = N // GW
    PB = 2
    CHUNK = 512
    RING = 4
    PPC = CHUNK // (PB * P)
    K = RING * PPC
    BODY = K * PB
    IT = NB // BODY
    PG = NB // PB
    LOOK = 5
    PADW = LOOK * PB * P
    GC = 2 * DH + 1
    STEP_W = PB * GW
    NF = 4

    adj_rows = adj.rearrange("(b p) n -> p b n", p=P)
    x_rows = x.rearrange("(b p) d -> p b d", p=P)
    out_rows = out.rearrange("(b p) d -> p b d", p=P)
    adj_diag = bass.AP(adj.tensor, 0, [[N + 1, P], [(N + 1) * P, NB]])

    ctx = ExitStack()
    with ctx:
        def sb(name, shape, dt):
            return ctx.enter_context(nc.sbuf_tensor(name, shape, dt))

        def pb(name, shape, dt):
            return ctx.enter_context(nc.psum_tensor(name, shape, dt))

        def sem(name):
            return ctx.enter_context(nc.semaphore(name))

        ctx.enter_context(nc.allow_non_contiguous_dma(reason="bias columns and the diagonal of adj"))

        res = sb("res", [P, NB, D], F32)
        hx_hi = sb("hx_hi", [P, N + PADW], F16)
        hx_lo = sb("hx_lo", [P, N + PADW], F16)
        g = sb("g", [P, NB, GC], F16)
        diag_fix = sb("diag_fix", [P, NB, DH + 1], F32)
        ring = sb("ring", [P, RING, GB, CHUNK], F32)
        ident_bf = sb("ident_bf", [P, P], BF16)
        ident_f = sb("ident_f", [P, P], F32)
        zeros = sb("zeros", [P, 2 * GC], F16)
        half = sb("half", [P, GB], F32)
        exp_bias = sb("exp_bias", [P, 1], F32)
        work = sb("work", [P, (2 + 2 * NF) * STEP_W], F32)
        xt = work[:, 0:N]
        tanh_b = [work[:, b * STEP_W:(b + 1) * STEP_W] for b in range(2)]
        f_b = [work[:, (2 + b) * STEP_W:(3 + b) * STEP_W] for b in range(NF)]
        p_b = [work[:, (2 + NF + b) * STEP_W:(3 + NF + b) * STEP_W] for b in range(NF)]
        wt = sb("wt", [P, D], F32)
        w12 = sb("w12", [P, 2 * DH], F32)
        b12 = sb("b12", [P, GB, 2 * DH], F32)
        cols = sb("cols", [P, 8], F32)
        gam, bet, btc, bts, bn_a, bn_b, one, neg_m = (cols[:, i:i + 1] for i in range(8))
        stats = sb("stats", [P, NG, 6], F32)
        mv = sb("mv", [P, 2], F32)
        hx_f = sb("hx_f", [P, 2, GW], F32)
        hx_sq = sb("hx_sq", [P, 2, GW], F32)
        og = sb("og", [P, 2, GB, 2 * DH], F32)
        leak = sb("leak", [P, GB, DH], F32)
        adj_ii = sb("adj_ii", [P, NB], F32)
        f_ii = sb("f_ii", [P, 2, NB], F32)
        acc_s = sb("acc_s", [P, GB, DH + 1], F32)
        rden = sb("rden", [P, GB], F32)
        att = sb("att", [P, GB, DH], F32)
        att2 = sb("att2", [P, GB, DH], F32)
        cent = sb("cent", [P, GB, D], F32)
        sq = sb("sq", [P, GB, D], F32)
        mean = sb("mean", [P, GB], F32)
        var = sb("var", [P, GB], F32)

        scores = [pb(f"scores{i}", [P, STEP_W], F32) for i in range(2)]
        adj_t = [pb(f"adj_t{i}", [P, STEP_W], BF16) for i in range(2)]
        acc = [pb(f"acc{i}", [P, 512], F32) for i in range(2)]
        bank = [scores[i][:, j * 512:(j + 1) * 512] for i in range(2) for j in range(2)]
        s_ii = acc[0][:, 0:NB]

        par_loaded = sem("par_loaded")
        x_loaded = [sem(f"x_loaded{i}") for i in range(4)]
        diag_loaded = sem("diag_loaded")
        const_made = sem("const_made")
        xt_ready, xt_copied, stats_made = sem("xt_ready"), sem("xt_copied"), sem("stats_made")
        bn_step, rstd_made, hn_made = sem("bn_step"), sem("rstd_made"), sem("hn_made")
        hx_ready, hxf_made, hxsq_made, hi_made, lo_made = (sem("hx_ready"), sem("hxf_made"), sem("hxsq_made"),
                                                           sem("hi_made"), sem("lo_made"))
        og_ready, og_made, gfull_made, ghi_made, glo_made, out1_step = (
            sem("og_ready"), sem("og_made"), sem("gfull_made"), sem("ghi_made"), sem("glo_made"), sem("out1_step"))
        dots_done, fii_step, fix_step, pro_done = sem("dots_done"), sem("fii_step"), sem("fix_step"), sem("pro_done")
        adj_loaded = [sem(f"adj_loaded{i}") for i in range(RING)]
        scores_ready = sem("scores_ready")
        tanh_done = sem("tanh_done")
        exp_done = sem("exp_done")
        split_done = sem("split_done")
        adjt_ready = sem("adjt_ready")
        masked = sem("masked")
        f_free = sem("f_free")
        p_free = sem("p_free")
        sums_step = sem("sums_step")
        rden_made = sem("rden_made")
        epi_step = sem("epi_step")
        epi_turn = sem("epi_turn")
        stored = sem("stored")

        block = ctx.enter_context(nc.Block())
        EPI = 12 + 2 * int(math.log2(D))

        NPAR = 5 + 2 + 2 * GB

        @block.sync
        def _(sp):
            XQ = NB // 4
            for i in range(4):
                sp.dma_start(res[:, i * XQ:(i + 1) * XQ, :], x_rows[:, i * XQ:(i + 1) * XQ, :]).then_inc(x_loaded[i], 16)
            col = lambda v: v.rearrange("(p o) -> p o", o=1)
            row = lambda v: v.rearrange("(o n) -> o n", o=1).to_broadcast([P, DH])
            for dst, src in ((gam, col(gamma)), (bet, col(beta)), (btc, col(bt)), (wt[:, :], Wt),
                             (w12[:, 0:DH], W1), (w12[:, DH:2 * DH], W2)):
                sp.dma_start(dst, src).then_inc(par_loaded, 16)
            for r in range(GB):
                sp.dma_start(b12[:, r, 0:DH], row(b1)).then_inc(par_loaded, 16)
                sp.dma_start(b12[:, r, DH:2 * DH], row(b2)).then_inc(par_loaded, 16)
            for c in range(RING):
                sp.dma_start(ring[:, c, :, :], adj_rows[:, 0:GB, c * CHUNK:(c + 1) * CHUNK]).then_inc(adj_loaded[c], 16)
            sp.dma_start(adj_ii[:, :], adj_diag).then_inc(diag_loaded, 16)
            with sp.Fori(1, IT) as it:
                for c in range(RING):
                    sp.wait_ge(adjt_ready, (it - 1) * K + (c + 1) * PPC)
                    sp.dma_start(ring[:, c, :, :],
                                 adj_rows[:, 0:GB, bass.ds(it * (RING * CHUNK) + c * CHUNK, CHUNK)]
                                 ).then_inc(adj_loaded[c], 16)
            with sp.Fori(1, NG) as s:
                with sp.Fori(0, IT) as it:
                    for c in range(RING):
                        sp.wait_ge(adjt_ready, (s * IT + it - 1) * K + (c + 1) * PPC)
                        sp.dma_start(ring[:, c, :, :],
                                     adj_rows[:, bass.ds(s * GB, GB), bass.ds(it * (RING * CHUNK) + c * CHUNK, CHUNK)]
                                     ).then_inc(adj_loaded[c], 16)
            sp.wait_ge(adjt_ready, (NG * IT - 1) * K + PPC)
            sp.sem_inc(adj_loaded[0], 16)

        @block.gpsimd
        def _(pool):
            nc.gpsimd.memset(ident_f[:, :], 0.0).then_inc(const_made, 1)
            nc.gpsimd.memset(ident_bf[:, :], 0.0).then_inc(const_made, 1)
            pool.wait_ge(const_made, 2)
            for m in (ident_f, ident_bf):
                nc.gpsimd.affine_select(out=m[:, :], in_=m[:, :], compare_op=ALU.not_equal, fill=1.0,
                                        base=0, pattern=[[-1, P]], channel_multiplier=1).then_inc(const_made, 1)
            nc.gpsimd.memset(zeros[:, :], 0.0).then_inc(const_made, 1)
            nc.gpsimd.memset(one, 1.0).then_inc(const_made, 1)
            nc.gpsimd.memset(half[:, :], -0.5).then_inc(const_made, 1)
            nc.gpsimd.memset(exp_bias[:, :], math.log(PS) - 0.5).then_inc(const_made, 1)
            nc.gpsimd.memset(g[:, :, DH:DH + 1], GS).then_inc(const_made, 1)
            nc.gpsimd.memset(diag_fix[:, :, DH:DH + 1], GS).then_inc(const_made, 1)
            pool.wait_ge(const_made, 10)
            pool.wait_ge(bn_step, 2)
            nc.gpsimd.tensor_tensor(bn_a, mv[:, 1:2], half[:, 0:1], ALU.pow).then_inc(rstd_made, 1)
            for i in range(NG):
                pool.wait_ge(og_made, i + 1)
                if i:
                    pool.wait_ge(out1_step, 4 * i)
                h1 = og[:, i % 2, :, 0:DH]
                dst = res[:, i * GB:(i + 1) * GB, 0:DH]
                nc.gpsimd.tensor_scalar(leak[:, :, :], h1, 0.0, LEAKY, ALU.min, ALU.mult).then_inc(out1_step, 1)
                nc.gpsimd.tensor_scalar(att[:, :, :], h1, 0.0, None, ALU.max).then_inc(out1_step, 1)
                pool.wait_ge(out1_step, 4 * i + 2)
                nc.gpsimd.tensor_tensor(leak[:, :, :], leak[:, :, :], att[:, :, :], ALU.add).then_inc(out1_step, 1)
                pool.wait_ge(out1_step, 4 * i + 3)
                nc.gpsimd.tensor_tensor(dst, dst, leak[:, :, :], ALU.add).then_inc(out1_step, 1)
            pool.wait_ge(out1_step, 4 * NG)
            with pool.Fori(0, NG) as s:
                def bc(v, w):
                    return v.rearrange("p (b o) -> p b o", o=1).to_broadcast([P, GB, w])

                rows = res[:, bass.ds(s * GB, GB), :]
                lower = res[:, bass.ds(s * GB, GB), DH:D]
                n = [0]

                def then(ins):
                    n[0] += 1
                    ins.then_inc(epi_step, 1)
                    pool.wait_ge(epi_step, s * EPI + n[0])
                    pool.sem_inc(epi_turn, 1)

                def row_sums(src, dst):
                    w = D // 2
                    while w:
                        then(nc.gpsimd.tensor_tensor(dst[:, :, 0:w], src[:, :, 0:w], src[:, :, w:2 * w], ALU.add))
                        src, w = dst, w // 2

                pool.wait_ge(rden_made, s + 1)
                pool.sem_inc(epi_turn, 1)
                then(nc.gpsimd.tensor_tensor(att[:, :, :], acc_s[:, :, 0:DH], bc(rden[:, :], DH), ALU.mult))
                then(nc.gpsimd.tensor_scalar(att2[:, :, :], att[:, :, :], 0.0, LEAKY, ALU.min, ALU.mult))
                then(nc.gpsimd.tensor_scalar(att[:, :, :], att[:, :, :], 0.0, None, ALU.max))
                then(nc.gpsimd.tensor_tensor(att[:, :, :], att[:, :, :], att2[:, :, :], ALU.add))
                then(nc.gpsimd.tensor_tensor(lower, lower, att[:, :, :], ALU.add))
                row_sums(rows, cent)
                then(nc.gpsimd.tensor_scalar(mean[:, :], cent[:, :, 0], 1.0 / D, None, ALU.mult))
                then(nc.gpsimd.tensor_tensor(cent[:, :, :], rows, bc(mean[:, :], D), ALU.subtract))
                then(nc.gpsimd.tensor_tensor(sq[:, :, :], cent[:, :, :], cent[:, :, :], ALU.mult))
                row_sums(sq, sq)
                then(nc.gpsimd.tensor_scalar(var[:, :], sq[:, :, 0], 1.0 / D, LN_EPS, ALU.mult, ALU.add))
                then(nc.gpsimd.tensor_tensor(var[:, :], var[:, :], half[:, :], ALU.pow))
                then(nc.gpsimd.tensor_tensor(rows, cent[:, :, :], bc(var[:, :], D), ALU.mult))
                n[0] += 1
                pool.sem_inc(epi_step, 1)
                assert n[0] == EPI
                pool.dma_start(out_rows[:, bass.ds(s * GB, GB), :], rows).then_inc(stored, 16)
            pool.wait_ge(stored, 16 * NG)

        @block.scalar
        def _(act):
            for i in range(NG):
                act.wait_ge(xt_ready, i + 1)
                nc.scalar.copy(xt[:, i * GW:(i + 1) * GW], bank[i % 4]).then_inc(xt_copied, 1)
            act.wait_ge(bn_step, 5)
            for i in range(NG):
                act.wait_ge(hx_ready, i + 1)
                if i >= 2:
                    act.wait_ge(lo_made, i - 1)
                nc.scalar.activation(hx_f[:, i % 2, :], bank[i % 2], ACT.Identity, bias=bts, scale=HS).then_inc(hxf_made, 1)
                act.wait_ge(hxf_made, i + 1)
                if i >= 2:
                    act.wait_ge(dots_done, i - 1)
                nc.scalar.activation(hx_sq[:, i % 2, :], hx_f[:, i % 2, :], ACT.Square, scale=1.0 / HS).then_inc(hxsq_made, 1)
                act.wait_ge(og_made, i + 1)
                blocks = slice(i * GB, (i + 1) * GB)
                g_in = og[:, i % 2, :, DH:2 * DH]
                nc.scalar.mul(diag_fix[:, blocks, 0:DH], g_in, GS).then_inc(gfull_made, 1)
                nc.scalar.mul(g[:, blocks, 0:DH], g_in, GS).then_inc(ghi_made, 1)
            act.wait_ge(dots_done, NG)
            nc.scalar.activation(f_ii[:, 0, :], s_ii, ACT.Tanh, scale=0.5).then_inc(fii_step, 1)
            act.wait_ge(fii_step, 1)
            nc.scalar.activation(f_ii[:, 1, :], f_ii[:, 0, :], ACT.Exp, scale=0.5, bias=exp_bias[:, :]).then_inc(fii_step, 1)

            def tanh(q, b):
                act.wait_ge(scores_ready, q + 1)
                nc.scalar.activation(tanh_b[b], scores[b][:, :], ACT.Tanh, scale=0.5 / (HS * HS)).then_inc(tanh_done, 1)

            def expo(q, k):
                act.wait_ge(tanh_done, q + 1)
                act.wait_ge(f_free, q + 1)
                nc.scalar.activation(f_b[k % NF], tanh_b[k % 2], ACT.Exp, scale=0.5, bias=exp_bias[:, :]).then_inc(exp_done, 1)

            tanh(0, 0)
            with act.Fori(0, NG * IT) as n:
                for k in range(K):
                    act.wait_ge(exp_done, n * K + k)
                    tanh(n * K + k + 1, (k + 1) % 2)
                    expo(n * K + k, k)
            expo(NG * PG, 0)
            act.wait_ge(tanh_done, NG * PG + 1)
            act.sem_inc(tanh_done, LOOK - 3)

        @block.vector
        def _(dve):
            dve.sem_inc(f_free, NF)
            for i in range(NG):
                dve.wait_ge(xt_copied, i + 1)
                nc.vector.bn_stats(stats[:, i, :], xt[:, i * GW:(i + 1) * GW]).then_inc(stats_made, 1)
            dve.wait_ge(stats_made, NG)
            nc.vector.bn_aggr(mv[:, :], stats[:, :, :]).then_inc(bn_step, 1)
            dve.wait_ge(bn_step, 1)
            nc.vector.tensor_scalar(mv[:, 1:2], mv[:, 1:2], BN_EPS, None, ALU.add).then_inc(bn_step, 1)
            dve.wait_ge(rstd_made, 1)
            dve.wait_ge(par_loaded, 16 * (6 + 2 * GB))
            nc.vector.tensor_tensor(bn_a, bn_a, gam, ALU.mult).then_inc(bn_step, 1)
            dve.wait_ge(bn_step, 3)
            nc.vector.scalar_tensor_tensor(out=bn_b, in0=mv[:, 0:1], scalar=bn_a, in1=bet,
                                           op0=ALU.mult, op1=ALU.subtract).then_inc(bn_step, 1)
            nc.vector.tensor_scalar(bts, btc, HS, None, ALU.mult).then_inc(bn_step, 1)
            dve.wait_ge(bn_step, 5)
            for i in range(NG):
                c = xt[:, i * GW:(i + 1) * GW]
                nc.vector.tensor_scalar(c, c, bn_a, bn_b, ALU.mult, ALU.subtract).then_inc(hn_made, 1)
            for i in range(NG):
                c = slice(i * GW, (i + 1) * GW)
                dve.wait_ge(hxf_made, i + 1)
                nc.vector.tensor_copy(hx_hi[:, c], hx_f[:, i % 2, :]).then_inc(hi_made, 1)
                dve.wait_ge(og_ready, i + 1)
                if i >= 2:
                    dve.wait_ge(ghi_made, i - 1)
                    dve.wait_ge(out1_step, 4 * (i - 1))
                nc.vector.tensor_tensor(og[:, i % 2, :, :], bank[2 + i % 2].rearrange("p (b n) -> p b n", b=GB),
                                        b12[:, :, :], ALU.add).then_inc(og_made, 1)
                dve.wait_ge(hi_made, i + 1)
                nc.vector.tensor_tensor(hx_lo[:, c], hx_f[:, i % 2, :], hx_hi[:, c], ALU.subtract).then_inc(lo_made, 1)
                dve.wait_ge(gfull_made, i + 1)
                dve.wait_ge(ghi_made, i + 1)
                dve.wait_ge(const_made, 10)
                b = slice(i * GB, (i + 1) * GB)
                nc.vector.tensor_tensor(g[:, b, DH + 1:GC], diag_fix[:, b, 0:DH], g[:, b, 0:DH],
                                        ALU.subtract).then_inc(glo_made, 1)
            dve.wait_ge(hi_made, NG)
            dve.wait_ge(lo_made, NG)
            nc.vector.tensor_copy(hx_hi[:, N:N + PADW], hx_hi[:, 0:PADW]).then_inc(hi_made, 1)
            nc.vector.tensor_copy(hx_lo[:, N:N + PADW], hx_lo[:, 0:PADW]).then_inc(lo_made, 1)
            dve.wait_ge(fii_step, 2)
            dve.wait_ge(diag_loaded, 16)
            nc.vector.scalar_tensor_tensor(out=f_ii[:, 0, :], in0=adj_ii[:, :], scalar=0.0, in1=f_ii[:, 1, :],
                                           op0=ALU.is_gt, op1=ALU.mult).then_inc(fix_step, 1)
            dve.wait_ge(fix_step, 1)
            nc.vector.tensor_scalar(adj_ii[:, :], f_ii[:, 0, :], -1.0, PS, ALU.mult, ALU.add).then_inc(fix_step, 1)
            dve.wait_ge(fix_step, 2)
            dve.wait_ge(glo_made, NG)
            nc.vector.tensor_tensor(diag_fix[:, :, :], diag_fix[:, :, :],
                                    adj_ii[:, :].rearrange("p (b o) -> p b o", o=1).to_broadcast([P, NB, DH + 1]),
                                    ALU.mult).then_inc(fix_step, 1)
            dve.wait_ge(fix_step, 3)

            def split(q, k):
                dve.wait_ge(exp_done, q + 1)
                f = f_b[k % NF]
                nc.vector.tensor_tensor(f.bitcast(F16)[:, 0::2], f, f.bitcast(BF16)[:, 1::2],
                                        ALU.subtract).then_inc(split_done, 1)

            def mask(q, k):
                dve.wait_ge(split_done, q + 1)
                dve.wait_ge(adjt_ready, q + 1)
                dve.wait_ge(p_free, q + 1)
                nc.vector.scalar_tensor_tensor(out=p_b[k % NF], in0=adj_t[k % 2][:, :], scalar=0.0, in1=f_b[k % NF],
                                               op0=ALU.is_gt, op1=ALU.mult).then_inc(f_free, 1)

            split(0, 0)
            with dve.Fori(0, NG) as s:
                with dve.Fori(0, IT) as it:
                    for k in range(K):
                        q = (s * IT + it) * K + k
                        split(q + 1, k + 1)
                        mask(q, k)
                dve.wait_ge(p_free, (s + 1) * PG + NF)
                dve.wait_ge(epi_step, s * EPI)
                for h in range(2):
                    a = acc[h][:, 0:2 * GC].rearrange("p (b n) -> p b n", b=2)
                    nc.vector.tensor_tensor(acc_s[:, 2 * h:2 * h + 2, :], a[:, :, 0:DH + 1],
                                            diag_fix[:, bass.ds(s * GB + 2 * h, 2), :], ALU.add).then_inc(sums_step, 1)
                dve.wait_ge(sums_step, s * 4 + 2)
                for h in range(2):
                    a = acc[h][:, 0:2 * GC].rearrange("p (b n) -> p b n", b=2)
                    o = acc_s[:, 2 * h:2 * h + 2, 0:DH]
                    nc.vector.tensor_tensor(o, o, a[:, :, DH + 1:GC], ALU.add).then_inc(sums_step, 1)
                dve.wait_ge(sums_step, s * 4 + 4)
                nc.vector.reciprocal(rden[:, :].rearrange("p (b o) -> p b o", o=1),
                                     acc_s[:, :, DH:DH + 1]).then_inc(rden_made, 1)

        @block.tensor
        def _(pe):
            pe.sem_inc(p_free, NF)
            pe.wait_ge(const_made, 10)
            for i in range(NG):
                if i % 4 == 0:
                    pe.wait_ge(x_loaded[i // 4], 16)
                if i >= 4:
                    pe.wait_ge(xt_copied, i - 3)
                for b in range(GB):
                    t = nc.tensor.transpose(bank[i % 4][:, b * P:(b + 1) * P], res[:, i * GB + b, :], ident_f[:, :])
                t.then_inc(xt_ready, 1)
            pe.wait_ge(par_loaded, 16 * (6 + 2 * GB))
            pe.wait_ge(xt_copied, NG)
            for i in range(NG + 1):
                if i < NG:
                    pe.wait_ge(hn_made, i + 1)
                    if i >= 2:
                        pe.wait_ge(hxf_made, i - 1)
                    c = xt[:, i * GW:(i + 1) * GW]
                    nc.tensor.matmul(bank[i % 2], wt[:, :], c, start=True, stop=True).then_inc(hx_ready, 1)
                    if i >= 2:
                        pe.wait_ge(og_made, i - 1)
                    for b in range(GB):
                        m = nc.tensor.matmul(bank[2 + i % 2][:, b * P:(b + 1) * P], c[:, b * P:(b + 1) * P], w12[:, :],
                                             start=True, stop=True)
                    m.then_inc(og_ready, 1)
                if i:
                    pe.wait_ge(hxsq_made, i)
                    for b in range(GB):
                        blk = (i - 1) * GB + b
                        m = nc.tensor.matmul(s_ii[:, blk:blk + 1], hx_sq[:, (i - 1) % 2, b * P:(b + 1) * P], one,
                                             start=True, stop=True)
                    m.then_inc(dots_done, 1)
            pe.wait_ge(hi_made, NG + 1)
            pe.wait_ge(lo_made, NG + 1)
            pe.wait_ge(glo_made, NG)
            pe.wait_ge(hxf_made, NG)
            pe.wait_ge(og_made, NG)
            pe.wait_ge(fii_step, 1)

            def make_scores(q, k, jcol, icol, fresh=False):
                if not fresh:
                    pe.wait_ge(tanh_done, q - 1)
                for t in range(PB):
                    o = scores[k % 2][:, t * GW:(t + 1) * GW]
                    j = bass.ds(jcol + t * P, P)
                    i = bass.ds(icol, GW)
                    nc.tensor.matmul(o, hx_hi[:, j], hx_hi[:, i], start=True, stop=False)
                    nc.tensor.matmul(o, hx_hi[:, j], hx_lo[:, i], start=False, stop=False)
                    m = nc.tensor.matmul(o, hx_lo[:, j], hx_hi[:, i], start=False, stop=True)
                m.then_inc(scores_ready, 1)

            def transpose_adj(q, k, loads):
                c = (k // PPC) % RING
                pe.wait_ge(adj_loaded[c], 16 * loads)
                if q is not None:
                    pe.wait_ge(f_free, q - 1 + NF)
                upper = ring[:, c, :, :].bitcast(BF16)[:, :, 1::2]
                for t in range(PB):
                    for b in range(GB):
                        o = (t * GB + b) * P
                        col = ((k % PPC) * PB + t) * P
                        m = nc.tensor.transpose(adj_t[k % 2][:, o:o + P], upper[:, b, col:col + P], ident_bf[:, :])
                        if t == PB - 1 and b == GB - 1:
                            m.then_inc(adjt_ready, 1)
                return m

            def product(q, k, blk):
                pe.wait_ge(f_free, q + 1 + NF)
                p_hi = p_b[k % NF].bitcast(BF16)[:, 1::2]
                p_lo = p_b[k % NF].bitcast(F16)[:, 0::2]
                for t in range(PB):
                    for b in range(GB):
                        o = (t * GB + b) * P
                        a = acc[b // 2][:, (b % 2) * GC:(b % 2) * GC + GC]
                        nc.tensor.matmul(a, p_hi[:, o:o + P], g[:, bass.ds(blk + t, 1), :],
                                         start=False, stop=False, skip_group_check=True)
                        m = nc.tensor.matmul(a[:, 0:DH + 1], p_lo[:, o:o + P], g[:, bass.ds(blk + t, 1), 0:DH + 1],
                                             start=False, stop=True, skip_group_check=True)
                m.then_inc(p_free, 1)

            for k in range(LOOK):
                make_scores(k, k, k * PB * P, 0, fresh=k < 2)
            transpose_adj(None, 0, 1)
            with pe.Fori(0, NG) as s:
                pe.wait_ge(sums_step, s * 4)
                for h in range(2):
                    nc.tensor.matmul(acc[h][:, 0:2 * GC], zeros[:, 0:P], zeros[:, :], start=True, stop=False,
                                     skip_group_check=True)
                with pe.Fori(0, IT) as it:
                    n = s * IT + it
                    for k in range(K):
                        q = n * K + k
                        nk = k + 1
                        transpose_adj(q + 1, nk % K, n + 1 + nk // K)
                        product(q, k, it * BODY + k * PB)
                        lk = k + LOOK
                        jcol = it * (BODY * P) + lk * PB * P
                        icol = ((n + lk // K) // IT) * GW
                        make_scores(q + LOOK, lk, jcol, icol)


_INS = ['x', 'adj', 'L0_gnn_gamma', 'L0_gnn_beta', 'L0_gnn_Wt', 'L0_gnn_bt', 'L0_gnn_W1', 'L0_gnn_b1',
        'L0_gnn_W2', 'L0_gnn_b2']


def kernel(**inputs):
    import numpy as _np
    import concourse.bacc as _bacc
    from concourse import mybir as _mybir
    from concourse.bass_utils import run_bass_kernel_spmd as _run

    nc = _bacc.Bacc("TRN2", target_bir_lowering=False, num_devices=1)
    arrays, args = {}, []
    for name in _INS:
        a = _np.ascontiguousarray(inputs[name])
        arrays[f"in_{name}_dram"] = a
        args.append(nc.dram_tensor(f"in_{name}_dram", a.shape, _mybir.dt.from_np(a.dtype), kind="ExternalInput").ap())
    out = nc.dram_tensor("out_0_dram", inputs['x'].shape, _mybir.dt.float32, kind="ExternalOutput").ap()
    gnn_kernel(nc, *args, out)
    r = _run(nc, [arrays], core_ids=[0])
    return r.results[0]["out_0_dram"]
```

```python
import math
from contextlib import ExitStack

import concourse.bass as bass
from concourse import mybir

F32 = mybir.dt.float32
F16 = mybir.dt.float16
BF16 = mybir.dt.bfloat16
ALU = mybir.AluOpType
ACT = mybir.ActivationFunctionType
AX = mybir.AxisListType

BN_EPS = 1e-5
LN_EPS = 1e-5
LEAKY = 0.01
HS = 32.0
GS = 64.0
PS = 64.0

P = 128


def gnn_kernel(nc, x, adj, gamma, beta, Wt, bt, W1, b1, W2, b2, out):
    N, D = x.shape
    DH = W2.shape[1]
    NB = N // P
    GB = 4
    GW = GB * P
    NG = N // GW
    PB = 2
    CHUNK = 512
    RING = 4
    PPC = CHUNK // (PB * P)
    K = RING * PPC
    BODY = K * PB
    IT = NB // BODY
    PG = NB // PB
    LOOK = 5
    PADW = LOOK * PB * P
    GC = 2 * DH + 1
    STEP_W = PB * GW
    NF = 4
    SPLIT = 704

    adj_rows = adj.rearrange("(b p) n -> p b n", p=P)
    x_rows = x.rearrange("(b p) d -> p b d", p=P)
    out_rows = out.rearrange("(b p) d -> p b d", p=P)
    adj_diag = bass.AP(adj.tensor, 0, [[N + 1, P], [(N + 1) * P, NB]])

    ctx = ExitStack()
    with ctx:
        def sb(name, shape, dt):
            return ctx.enter_context(nc.sbuf_tensor(name, shape, dt))

        def pb(name, shape, dt):
            return ctx.enter_context(nc.psum_tensor(name, shape, dt))

        def sem(name):
            return ctx.enter_context(nc.semaphore(name))

        ctx.enter_context(nc.allow_non_contiguous_dma(reason="bias columns and the diagonal of adj"))

        res = sb("res", [P, NB, D], F32)
        hx_hi = sb("hx_hi", [P, N + PADW], F16)
        hx_lo = sb("hx_lo", [P, N + PADW], F16)
        g = sb("g", [P, NB, GC], F16)
        g_f = sb("g_f", [P, NB, DH + 1], F32)
        w_fix = sb("w_fix", [P, NB], F32)
        ring = sb("ring", [P, RING, GB, CHUNK], F32)
        ident_bf = sb("ident_bf", [P, P], BF16)
        ident_f = sb("ident_f", [P, P], F32)
        zeros = sb("zeros", [P, 2 * GC], F16)
        half = sb("half", [P, GB], F32)
        minus_one = sb("minus_one", [P, GB], F32)
        exp_bias = sb("exp_bias", [P, 1], F32)
        work = sb("work", [P, (2 + 2 * NF) * STEP_W], F32)
        xt = work[:, 0:N]
        tanh_b = [work[:, b * STEP_W:(b + 1) * STEP_W] for b in range(2)]
        f_b = [work[:, (2 + b) * STEP_W:(3 + b) * STEP_W] for b in range(NF)]
        p_b = [work[:, (2 + NF + b) * STEP_W:(3 + NF + b) * STEP_W] for b in range(NF)]
        wt = sb("wt", [P, D], F32)
        w12 = sb("w12", [P, 2 * DH], F32)
        b12 = sb("b12", [P, GB, 2 * DH], F32)
        cols = sb("cols", [P, 8], F32)
        gam, bet, btc, bts, bn_a, bn_b, one, neg_m = (cols[:, i:i + 1] for i in range(8))
        stats = sb("stats", [P, NG, 6], F32)
        mv = sb("mv", [P, 2], F32)
        hx_f = sb("hx_f", [P, 2, GW], F32)
        hx_sq = sb("hx_sq", [P, 2, GW], F32)
        og = sb("og", [P, 2, GB, 2 * DH], F32)
        leak = sb("leak", [P, 2, GB, DH], F32)
        adj_ii = sb("adj_ii", [P, NB], F32)
        f_ii = sb("f_ii", [P, 2, NB], F32)
        sums = sb("sums", [P, GB, GC], F32)
        acc_s = sb("acc_s", [P, GB, DH + 1], F32)
        fix = sb("fix", [P, GB, DH + 1], F32)
        rden = sb("rden", [P, GB], F32)
        att = sb("att", [P, GB, DH], F32)
        att2 = sb("att2", [P, GB, DH], F32)
        cent = sb("cent", [P, GB, D], F32)
        sq = sb("sq", [P, GB, D], F32)
        mean = sb("mean", [P, GB], F32)
        var = sb("var", [P, GB], F32)

        scores = [pb(f"scores{i}", [P, STEP_W], F32) for i in range(2)]
        adj_t = [pb(f"adj_t{i}", [P, STEP_W], BF16) for i in range(2)]
        acc = [pb(f"acc{i}", [P, 512], F32) for i in range(2)]
        bank = [scores[i][:, j * 512:(j + 1) * 512] for i in range(2) for j in range(2)]
        s_ii = acc[0][:, 0:NB]

        par_loaded = sem("par_loaded")
        x_loaded = [sem(f"x_loaded{i}") for i in range(4)]
        diag_loaded = sem("diag_loaded")
        const_made = sem("const_made")
        xt_ready, xt_copied, stats_made = sem("xt_ready"), sem("xt_copied"), sem("stats_made")
        bn_step, rstd_made, hn_made = sem("bn_step"), sem("rstd_made"), sem("hn_made")
        hx_ready, hxf_made, hxsq_made, hi_made, lo_made = (sem("hx_ready"), sem("hxf_made"), sem("hxsq_made"),
                                                           sem("hi_made"), sem("lo_made"))
        og_ready, og_made, gfull_made, ghi_made, glo_made, leaky_made, out1_made = (
            sem("og_ready"), sem("og_made"), sem("gfull_made"), sem("ghi_made"), sem("glo_made"),
            sem("leaky_made"), sem("out1_made"))
        dots_done, fii_step, fix_step, pro_done = sem("dots_done"), sem("fii_step"), sem("fix_step"), sem("pro_done")
        adj_loaded = [sem(f"adj_loaded{i}") for i in range(RING)]
        scores_ready = sem("scores_ready")
        tanh_done = sem("tanh_done")
        exp_done = sem("exp_done")
        split_done = sem("split_done")
        adjt_ready = sem("adjt_ready")
        masked = sem("masked")
        f_free = sem("f_free")
        p_free = sem("p_free")
        sums_copied = sem("sums_copied")
        epi_step = sem("epi_step")
        epi_turn = sem("epi_turn")
        stored = sem("stored")
        split_pool = sem("split_pool")
        last_step, last_rstd = sem("last_step"), sem("last_rstd")
        stored_last = sem("stored_last")

        START = 1

        block = ctx.enter_context(nc.Block())
        HALVINGS = int(math.log2(D))
        EPI = 15 + 2 * HALVINGS
        EPI_AT = 5
        SMALL = [at + h for at in (9, 12 + HALVINGS) for h in (4, 6)]
        LAST_STEPS = 17

        NPAR = 5 + 2 + 2 * GB

        @block.sync
        def _(sp):
            XQ = NB // 4
            for i in range(4):
                sp.dma_start(res[:, i * XQ:(i + 1) * XQ, :], x_rows[:, i * XQ:(i + 1) * XQ, :]).then_inc(x_loaded[i], 16)
            col = lambda v: v.rearrange("(p o) -> p o", o=1)
            row = lambda v: v.rearrange("(o n) -> o n", o=1).to_broadcast([P, DH])
            for dst, src in ((gam, col(gamma)), (bet, col(beta)), (btc, col(bt)), (wt[:, :], Wt),
                             (w12[:, 0:DH], W1), (w12[:, DH:2 * DH], W2)):
                sp.dma_start(dst, src).then_inc(par_loaded, 16)
            for r in range(GB):
                sp.dma_start(b12[:, r, 0:DH], row(b1)).then_inc(par_loaded, 16)
                sp.dma_start(b12[:, r, DH:2 * DH], row(b2)).then_inc(par_loaded, 16)
            for c in range(RING):
                sp.dma_start(ring[:, c, :, :], adj_rows[:, 0:GB, c * CHUNK:(c + 1) * CHUNK]).then_inc(adj_loaded[c], 16)
            sp.dma_start(adj_ii[:, :], adj_diag).then_inc(diag_loaded, 16)
            with sp.Fori(1, IT) as it:
                for c in range(RING):
                    sp.wait_ge(adjt_ready, (it - 1) * K + (c + 1) * PPC)
                    sp.dma_start(ring[:, c, :, :],
                                 adj_rows[:, 0:GB, bass.ds(it * (RING * CHUNK) + c * CHUNK, CHUNK)]
                                 ).then_inc(adj_loaded[c], 16)
            with sp.Fori(1, NG) as s:
                with sp.Fori(0, IT) as it:
                    for c in range(RING):
                        sp.wait_ge(adjt_ready, (s * IT + it - 1) * K + (c + 1) * PPC)
                        sp.dma_start(ring[:, c, :, :],
                                     adj_rows[:, bass.ds(s * GB, GB), bass.ds(it * (RING * CHUNK) + c * CHUNK, CHUNK)]
                                     ).then_inc(adj_loaded[c], 16)
            sp.wait_ge(adjt_ready, (NG * IT - 1) * K + PPC)
            sp.sem_inc(adj_loaded[0], 16)
            sp.wait_ge(last_step, LAST_STEPS + GB)
            sp.dma_start(out_rows[:, NB - GB:NB, :], res[:, NB - GB:NB, :]).then_inc(stored_last, 16)
            sp.wait_ge(stored_last, 16)

        @block.gpsimd
        def _(pool):
            pool.sem_inc(epi_step, START)
            nc.gpsimd.memset(ident_f[:, :], 0.0).then_inc(const_made, 1)
            nc.gpsimd.memset(ident_bf[:, :], 0.0).then_inc(const_made, 1)
            pool.wait_ge(const_made, 2)
            for m in (ident_f, ident_bf):
                nc.gpsimd.affine_select(out=m[:, :], in_=m[:, :], compare_op=ALU.not_equal, fill=1.0,
                                        base=0, pattern=[[-1, P]], channel_multiplier=1).then_inc(const_made, 1)
            nc.gpsimd.memset(zeros[:, :], 0.0).then_inc(const_made, 1)
            nc.gpsimd.memset(one, 1.0).then_inc(const_made, 1)
            nc.gpsimd.memset(half[:, :], -0.5).then_inc(const_made, 1)
            nc.gpsimd.memset(exp_bias[:, :], math.log(PS) - 0.5).then_inc(const_made, 1)
            nc.gpsimd.memset(g[:, :, DH:DH + 1], GS).then_inc(const_made, 1)
            nc.gpsimd.memset(g_f[:, :, DH:DH + 1], GS).then_inc(const_made, 1)
            nc.gpsimd.memset(minus_one[:, :], -1.0).then_inc(const_made, 1)
            pool.wait_ge(const_made, 11)
            pool.wait_ge(bn_step, 2)
            nc.gpsimd.tensor_tensor(bn_a, mv[:, 1:2], half[:, 0:1], ALU.pow).then_inc(rstd_made, 1)
            for i in range(NG):
                pool.wait_ge(leaky_made, i + 1)
                dst = res[:, i * GB:(i + 1) * GB, 0:DH]
                nc.gpsimd.tensor_tensor(dst, dst, leak[:, i % 2, :, :], ALU.add).then_inc(out1_made, 1)
            pool.wait_ge(out1_made, NG)
            def bc(v, w):
                return v.rearrange("p (b o) -> p b o", o=1).to_broadcast([P, GB, w])

            def split(q, k):
                pool.wait_ge(exp_done, q + 1 + START)
                f = f_b[k % NF][:, SPLIT:STEP_W]
                nc.gpsimd.tensor_tensor(f.bitcast(F16)[:, 0::2], f, f.bitcast(BF16)[:, 1::2],
                                        ALU.subtract).then_inc(split_pool, 1)

            def row_sums(src, dst):
                w = D // 2
                while w:
                    yield nc.gpsimd.tensor_tensor(dst[:, :, 0:w], src[:, :, 0:w], src[:, :, w:2 * w], ALU.add)
                    src, w = dst, w // 2

            def epilogue(rows, fixed, w):
                tt, ts = nc.gpsimd.tensor_tensor, nc.gpsimd.tensor_scalar
                lower = rows[:, :, DH:D]
                yield tt(fix[:, :, :], fixed, bc(w, DH + 1), ALU.mult)
                yield tt(acc_s[:, :, :], sums[:, :, 0:DH + 1], fix[:, :, :], ALU.add)
                yield tt(acc_s[:, :, 0:DH], acc_s[:, :, 0:DH], sums[:, :, DH + 1:GC], ALU.add)
                yield tt(rden[:, :], acc_s[:, :, DH], minus_one[:, :], ALU.pow)
                yield tt(att[:, :, :], acc_s[:, :, 0:DH], bc(rden[:, :], DH), ALU.mult)
                yield ts(att2[:, :, :], att[:, :, :], 0.0, LEAKY, ALU.min, ALU.mult)
                yield ts(att[:, :, :], att[:, :, :], 0.0, None, ALU.max)
                yield tt(att[:, :, :], att[:, :, :], att2[:, :, :], ALU.add)
                yield tt(lower, lower, att[:, :, :], ALU.add)
                yield from row_sums(rows, cent)
                yield ts(mean[:, :], cent[:, :, 0], 1.0 / D, None, ALU.mult)
                yield tt(cent[:, :, :], rows, bc(mean[:, :], D), ALU.subtract)
                yield tt(sq[:, :, :], cent[:, :, :], cent[:, :, :], ALU.mult)
                yield from row_sums(sq, sq)
                yield ts(var[:, :], sq[:, :, 0], 1.0 / D, LN_EPS, ALU.mult, ALU.add)
                yield tt(var[:, :], var[:, :], half[:, :], ALU.pow)
                yield tt(rows, cent[:, :, :], bc(var[:, :], D), ALU.mult)

            with pool.Fori(0, PG // NF) as n:
                for k in range(NF):
                    split(n * NF + k, k)
            with pool.Fori(1, NG) as s:
                rows = res[:, bass.ds(s * GB - GB, GB), :]
                steps = epilogue(rows, g_f[:, bass.ds(s * GB - GB, GB), :], w_fix[:, bass.ds(s * GB - GB, GB)])
                e = 0
                for k in range(PG):
                    split(s * PG + k, k)
                    while EPI_AT <= k and e <= EPI:
                        if e == 0:
                            pool.wait_ge(sums_copied, 2 * s + START)
                        else:
                            pool.wait_ge(epi_step, (s - 1) * EPI + e + START)
                        pool.sem_inc(epi_turn, 1)
                        if e < EPI:
                            next(steps).then_inc(epi_step, 1)
                        else:
                            pool.dma_start(out_rows[:, bass.ds(s * GB - GB, GB), :], rows).then_inc(stored, 16)
                        e += 1
                        if e not in SMALL:
                            break
                assert e == EPI + 1
            pool.wait_ge(last_step, LAST_STEPS)
            nc.gpsimd.tensor_tensor(var[:, :], var[:, :], half[:, :], ALU.pow).then_inc(last_rstd, 1)
            pool.wait_ge(stored, 16 * (NG - 1))

        @block.scalar
        def _(act):
            act.sem_inc(exp_done, START)
            act.sem_inc(sums_copied, START)
            for i in range(NG):
                act.wait_ge(xt_ready, i + 1)
                nc.scalar.copy(xt[:, i * GW:(i + 1) * GW], bank[i % 4]).then_inc(xt_copied, 1)
            act.wait_ge(bn_step, 5)

            def scale_g(i):
                act.wait_ge(og_made, i + 1)
                blocks = slice(i * GB, (i + 1) * GB)
                g_in = og[:, i % 2, :, DH:2 * DH]
                nc.scalar.mul(g_f[:, blocks, 0:DH], g_in, GS).then_inc(gfull_made, 1)
                nc.scalar.mul(g[:, blocks, 0:DH], g_in, GS).then_inc(ghi_made, 1)

            for i in range(NG):
                act.wait_ge(hx_ready, i + 1)
                if i >= 2:
                    act.wait_ge(lo_made, i - 1)
                nc.scalar.activation(hx_f[:, i % 2, :], bank[i % 2], ACT.Identity, bias=bts, scale=HS).then_inc(hxf_made, 1)
                act.wait_ge(hxf_made, i + 1)
                if i >= 2:
                    act.wait_ge(dots_done, i - 1)
                nc.scalar.activation(hx_sq[:, i % 2, :], hx_f[:, i % 2, :], ACT.Square, scale=1.0 / HS).then_inc(hxsq_made, 1)
                if i:
                    scale_g(i - 1)
            scale_g(NG - 1)
            act.wait_ge(dots_done, NG)
            nc.scalar.activation(f_ii[:, 0, :], s_ii, ACT.Tanh, scale=0.5).then_inc(fii_step, 1)
            act.wait_ge(fii_step, 1)
            nc.scalar.activation(f_ii[:, 1, :], f_ii[:, 0, :], ACT.Exp, scale=0.5, bias=exp_bias[:, :]).then_inc(fii_step, 1)

            def tanh(q, b):
                act.wait_ge(scores_ready, q + 1)
                nc.scalar.activation(tanh_b[b], scores[b][:, :], ACT.Tanh, scale=0.5 / (HS * HS)).then_inc(tanh_done, 1)

            def expo(q, k):
                act.wait_ge(tanh_done, q + 1)
                act.wait_ge(f_free, q + 1)
                nc.scalar.activation(f_b[k % NF], tanh_b[k % 2], ACT.Exp, scale=0.5, bias=exp_bias[:, :]).then_inc(exp_done, 1)

            def body(n, done=None):
                for k in range(K):
                    act.wait_ge(exp_done, n * K + k + START)
                    if done is not None and k == LOOK - 2:
                        copy_sums(done)
                    tanh(n * K + k + 1, (k + 1) % 2)
                    expo(n * K + k, k)

            def copy_sums(s):
                act.wait_ge(p_free, s * PG + NF)
                act.wait_ge(epi_step, (s - 1) * EPI + START)
                for h in range(2):
                    nc.scalar.copy(sums[:, 2 * h:2 * h + 2, :].rearrange("p b n -> p (b n)"),
                                   acc[h][:, 0:2 * GC]).then_inc(sums_copied, 1)

            tanh(0, 0)
            with act.Fori(0, IT) as it:
                body(it)
            with act.Fori(1, NG) as s:
                body(s * IT, done=s)
                with act.Fori(1, IT) as it:
                    body(s * IT + it)
            expo(NG * PG, 0)
            act.wait_ge(tanh_done, NG * PG + 1)
            act.sem_inc(tanh_done, LOOK - 3)
            copy_sums(NG)

        @block.vector
        def _(dve):
            dve.sem_inc(f_free, NF)
            for i in range(NG):
                dve.wait_ge(xt_copied, i + 1)
                nc.vector.bn_stats(stats[:, i, :], xt[:, i * GW:(i + 1) * GW]).then_inc(stats_made, 1)
            dve.wait_ge(stats_made, NG)
            nc.vector.bn_aggr(mv[:, :], stats[:, :, :]).then_inc(bn_step, 1)
            dve.wait_ge(bn_step, 1)
            nc.vector.tensor_scalar(mv[:, 1:2], mv[:, 1:2], BN_EPS, None, ALU.add).then_inc(bn_step, 1)
            dve.wait_ge(rstd_made, 1)
            dve.wait_ge(par_loaded, 16 * (6 + 2 * GB))
            nc.vector.tensor_tensor(bn_a, bn_a, gam, ALU.mult).then_inc(bn_step, 1)
            dve.wait_ge(bn_step, 3)
            nc.vector.scalar_tensor_tensor(out=bn_b, in0=mv[:, 0:1], scalar=bn_a, in1=bet,
                                           op0=ALU.mult, op1=ALU.subtract).then_inc(bn_step, 1)
            nc.vector.tensor_scalar(bts, btc, HS, None, ALU.mult).then_inc(bn_step, 1)
            dve.wait_ge(bn_step, 5)
            for i in range(NG):
                c = xt[:, i * GW:(i + 1) * GW]
                nc.vector.tensor_scalar(c, c, bn_a, bn_b, ALU.mult, ALU.subtract).then_inc(hn_made, 1)
            def low_of_g(i):
                dve.wait_ge(gfull_made, i + 1)
                dve.wait_ge(ghi_made, i + 1)
                b = slice(i * GB, (i + 1) * GB)
                nc.vector.tensor_tensor(g[:, b, DH + 1:GC], g_f[:, b, 0:DH], g[:, b, 0:DH],
                                        ALU.subtract).then_inc(glo_made, 1)

            dve.wait_ge(const_made, 11)
            for i in range(NG):
                c = slice(i * GW, (i + 1) * GW)
                dve.wait_ge(hxf_made, i + 1)
                nc.vector.tensor_copy(hx_hi[:, c], hx_f[:, i % 2, :]).then_inc(hi_made, 1)
                dve.wait_ge(og_ready, i + 1)
                if i >= 2:
                    dve.wait_ge(ghi_made, i - 1)
                    dve.wait_ge(leaky_made, i - 1)
                nc.vector.tensor_tensor(og[:, i % 2, :, :], bank[2 + i % 2].rearrange("p (b n) -> p b n", b=GB),
                                        b12[:, :, :], ALU.add).then_inc(og_made, 1)
                dve.wait_ge(hi_made, i + 1)
                nc.vector.tensor_tensor(hx_lo[:, c], hx_f[:, i % 2, :], hx_hi[:, c], ALU.subtract).then_inc(lo_made, 1)
                dve.wait_ge(og_made, i + 1)
                if i >= 2:
                    dve.wait_ge(out1_made, i - 1)
                h1 = og[:, i % 2, :, 0:DH]
                nc.vector.scalar_tensor_tensor(out=leak[:, i % 2, :, :], in0=h1, scalar=LEAKY, in1=h1,
                                               op0=ALU.mult, op1=ALU.max).then_inc(leaky_made, 1)
                if i >= 2:
                    low_of_g(i - 2)
            low_of_g(NG - 2)
            low_of_g(NG - 1)
            dve.wait_ge(hi_made, NG)
            dve.wait_ge(lo_made, NG)
            nc.vector.tensor_copy(hx_hi[:, N:N + PADW], hx_hi[:, 0:PADW]).then_inc(hi_made, 1)
            nc.vector.tensor_copy(hx_lo[:, N:N + PADW], hx_lo[:, 0:PADW]).then_inc(lo_made, 1)
            dve.wait_ge(fii_step, 2)
            dve.wait_ge(diag_loaded, 16)
            nc.vector.scalar_tensor_tensor(out=f_ii[:, 0, :], in0=adj_ii[:, :], scalar=0.0, in1=f_ii[:, 1, :],
                                           op0=ALU.is_gt, op1=ALU.mult).then_inc(fix_step, 1)
            dve.wait_ge(fix_step, 1)
            nc.vector.tensor_scalar(w_fix[:, :], f_ii[:, 0, :], -1.0, PS, ALU.mult, ALU.add).then_inc(fix_step, 1)

            def split(q, k):
                dve.wait_ge(exp_done, q + 1 + START)
                f = f_b[k % NF][:, 0:SPLIT]
                nc.vector.tensor_tensor(f.bitcast(F16)[:, 0::2], f, f.bitcast(BF16)[:, 1::2],
                                        ALU.subtract).then_inc(split_done, 1)

            def mask(q, k):
                dve.wait_ge(split_done, q + 1)
                dve.wait_ge(split_pool, q + 1)
                dve.wait_ge(adjt_ready, q + 1)
                dve.wait_ge(p_free, q + 1)
                nc.vector.scalar_tensor_tensor(out=p_b[k % NF], in0=adj_t[k % 2][:, :], scalar=0.0, in1=f_b[k % NF],
                                               op0=ALU.is_gt, op1=ALU.mult).then_inc(f_free, 1)

            split(0, 0)
            with dve.Fori(0, NG * IT) as n:
                for k in range(K):
                    split(n * K + k + 1, k + 1)
                    mask(n * K + k, k)

            n = [0]

            def then(ins):
                n[0] += 1
                ins.then_inc(last_step, 1)

            def bc(v, w):
                return v.rearrange("p (b o) -> p b o", o=1).to_broadcast([P, GB, w])

            rows = res[:, NB - GB:NB, :]
            lower = rows[:, :, DH:D]
            dve.wait_ge(sums_copied, 2 * NG + START)
            dve.wait_ge(epi_step, EPI * (NG - 1) + START)
            then(nc.vector.tensor_tensor(fix[:, :, :], g_f[:, NB - GB:NB, :], bc(w_fix[:, NB - GB:NB], DH + 1), ALU.mult))
            dve.wait_ge(last_step, n[0])
            then(nc.vector.tensor_tensor(acc_s[:, :, :], sums[:, :, 0:DH + 1], fix[:, :, :], ALU.add))
            dve.wait_ge(last_step, n[0])
            then(nc.vector.tensor_tensor(acc_s[:, :, 0:DH], acc_s[:, :, 0:DH], sums[:, :, DH + 1:GC], ALU.add))
            then(nc.vector.reciprocal(rden[:, :].rearrange("p (b o) -> p b o", o=1), acc_s[:, :, DH:DH + 1]))
            dve.wait_ge(last_step, n[0])
            then(nc.vector.tensor_tensor(att[:, :, :], acc_s[:, :, 0:DH], bc(rden[:, :], DH), ALU.mult))
            dve.wait_ge(last_step, n[0])
            then(nc.vector.scalar_tensor_tensor(out=att2[:, :, :], in0=att[:, :, :], scalar=LEAKY, in1=att[:, :, :],
                                                op0=ALU.mult, op1=ALU.max))
            dve.wait_ge(last_step, n[0])
            then(nc.vector.tensor_tensor(lower, lower, att2[:, :, :], ALU.add))
            dve.wait_ge(last_step, n[0])
            for b in range(GB):
                then(nc.vector.bn_stats(stats[:, b, :], rows[:, b, :]))
            dve.wait_ge(last_step, n[0])
            for b in range(GB):
                then(nc.vector.bn_aggr(stats[:, GB + b, 0:2], stats[:, b, :]))
            dve.wait_ge(last_step, n[0])
            then(nc.vector.tensor_scalar(var[:, :].rearrange("p (b o) -> p b o", o=1), stats[:, GB:2 * GB, 1:2],
                                         LN_EPS, None, ALU.add))
            then(nc.vector.tensor_copy(mean[:, :].rearrange("p (b o) -> p b o", o=1), stats[:, GB:2 * GB, 0:1]))
            assert n[0] == LAST_STEPS
            dve.wait_ge(last_step, n[0])
            dve.wait_ge(last_rstd, 1)
            for b in range(GB):
                then(nc.vector.tensor_scalar(rows[:, b, :], rows[:, b, :], mean[:, b:b + 1], var[:, b:b + 1],
                                             ALU.subtract, ALU.mult))

        @block.tensor
        def _(pe):
            pe.sem_inc(p_free, NF)
            pe.wait_ge(const_made, 10)
            for i in range(NG):
                if i % 4 == 0:
                    pe.wait_ge(x_loaded[i // 4], 16)
                if i >= 4:
                    pe.wait_ge(xt_copied, i - 3)
                for b in range(GB):
                    t = nc.tensor.transpose(bank[i % 4][:, b * P:(b + 1) * P], res[:, i * GB + b, :], ident_f[:, :])
                t.then_inc(xt_ready, 1)
            pe.wait_ge(par_loaded, 16 * (6 + 2 * GB))
            pe.wait_ge(xt_copied, NG)
            for i in range(NG + 1):
                if i < NG:
                    pe.wait_ge(hn_made, i + 1)
                    if i >= 2:
                        pe.wait_ge(hxf_made, i - 1)
                    c = xt[:, i * GW:(i + 1) * GW]
                    nc.tensor.matmul(bank[i % 2], wt[:, :], c, start=True, stop=True).then_inc(hx_ready, 1)
                    if i >= 2:
                        pe.wait_ge(og_made, i - 1)
                    for b in range(GB):
                        m = nc.tensor.matmul(bank[2 + i % 2][:, b * P:(b + 1) * P], c[:, b * P:(b + 1) * P], w12[:, :],
                                             start=True, stop=True)
                    m.then_inc(og_ready, 1)
                if i:
                    pe.wait_ge(hxsq_made, i)
                    for b in range(GB):
                        blk = (i - 1) * GB + b
                        m = nc.tensor.matmul(s_ii[:, blk:blk + 1], hx_sq[:, (i - 1) % 2, b * P:(b + 1) * P], one,
                                             start=True, stop=True)
                    m.then_inc(dots_done, 1)
            pe.wait_ge(hi_made, NG + 1)
            pe.wait_ge(lo_made, NG + 1)
            pe.wait_ge(glo_made, NG)
            pe.wait_ge(hxf_made, NG)
            pe.wait_ge(og_made, NG)
            pe.wait_ge(fii_step, 1)

            def make_scores(q, k, jcol, icol, fresh=False):
                if not fresh:
                    pe.wait_ge(tanh_done, q - 1)
                for t in range(PB):
                    o = scores[k % 2][:, t * GW:(t + 1) * GW]
                    j = bass.ds(jcol + t * P, P)
                    i = bass.ds(icol, GW)
                    nc.tensor.matmul(o, hx_hi[:, j], hx_hi[:, i], start=True, stop=False)
                    nc.tensor.matmul(o, hx_hi[:, j], hx_lo[:, i], start=False, stop=False)
                    m = nc.tensor.matmul(o, hx_lo[:, j], hx_hi[:, i], start=False, stop=True)
                m.then_inc(scores_ready, 1)

            def transpose_adj(q, k, loads):
                c = (k // PPC) % RING
                pe.wait_ge(adj_loaded[c], 16 * loads)
                if q is not None:
                    pe.wait_ge(f_free, q - 1 + NF)
                upper = ring[:, c, :, :].bitcast(BF16)[:, :, 1::2]
                for t in range(PB):
                    for b in range(GB):
                        o = (t * GB + b) * P
                        col = ((k % PPC) * PB + t) * P
                        m = nc.tensor.transpose(adj_t[k % 2][:, o:o + P], upper[:, b, col:col + P], ident_bf[:, :])
                        if t == PB - 1 and b == GB - 1:
                            m.then_inc(adjt_ready, 1)
                return m

            def product(q, k, blk):
                pe.wait_ge(f_free, q + 1 + NF)
                p_hi = p_b[k % NF].bitcast(BF16)[:, 1::2]
                p_lo = p_b[k % NF].bitcast(F16)[:, 0::2]
                for t in range(PB):
                    for b in range(GB):
                        o = (t * GB + b) * P
                        a = acc[b // 2][:, (b % 2) * GC:(b % 2) * GC + GC]
                        nc.tensor.matmul(a, p_hi[:, o:o + P], g[:, bass.ds(blk + t, 1), :],
                                         start=False, stop=False, skip_group_check=True)
                        m = nc.tensor.matmul(a[:, 0:DH + 1], p_lo[:, o:o + P], g[:, bass.ds(blk + t, 1), 0:DH + 1],
                                             start=False, stop=True, skip_group_check=True)
                m.then_inc(p_free, 1)

            for k in range(LOOK):
                make_scores(k, k, k * PB * P, 0, fresh=k < 2)
            transpose_adj(None, 0, 1)
            with pe.Fori(0, NG) as s:
                pe.wait_ge(sums_copied, s * 2 + START)
                for h in range(2):
                    nc.tensor.matmul(acc[h][:, 0:2 * GC], zeros[:, 0:P], zeros[:, :], start=True, stop=False,
                                     skip_group_check=True)
                with pe.Fori(0, IT) as it:
                    n = s * IT + it
                    for k in range(K):
                        q = n * K + k
                        nk = k + 1
                        transpose_adj(q + 1, nk % K, n + 1 + nk // K)
                        product(q, k, it * BODY + k * PB)
                        lk = k + LOOK
                        jcol = it * (BODY * P) + lk * PB * P
                        icol = ((n + lk // K) // IT) * GW
                        make_scores(q + LOOK, lk, jcol, icol)


_INS = ['x', 'adj', 'L0_gnn_gamma', 'L0_gnn_beta', 'L0_gnn_Wt', 'L0_gnn_bt', 'L0_gnn_W1', 'L0_gnn_b1',
        'L0_gnn_W2', 'L0_gnn_b2']


def kernel(**inputs):
    import numpy as _np
    import concourse.bacc as _bacc
    from concourse import mybir as _mybir
    from concourse.bass_utils import run_bass_kernel_spmd as _run

    nc = _bacc.Bacc("TRN2", target_bir_lowering=False, num_devices=1)
    arrays, args = {}, []
    for name in _INS:
        a = _np.ascontiguousarray(inputs[name])
        arrays[f"in_{name}_dram"] = a
        args.append(nc.dram_tensor(f"in_{name}_dram", a.shape, _mybir.dt.from_np(a.dtype), kind="ExternalInput").ap())
    out = nc.dram_tensor("out_0_dram", inputs['x'].shape, _mybir.dt.float32, kind="ExternalOutput").ap()
    gnn_kernel(nc, *args, out)
    r = _run(nc, [arrays], core_ids=[0])
    return r.results[0]["out_0_dram"]
```

```python
import math
from contextlib import ExitStack

import concourse.bass as bass
from concourse import mybir

F32 = mybir.dt.float32
F16 = mybir.dt.float16
BF16 = mybir.dt.bfloat16
ALU = mybir.AluOpType
ACT = mybir.ActivationFunctionType
AX = mybir.AxisListType

BN_EPS = 1e-5
LN_EPS = 1e-5
LEAKY = 0.01
HS = 32.0
GS = 64.0
PS = 64.0

P = 128


def gnn_kernel(nc, x, adj, gamma, beta, Wt, bt, W1, b1, W2, b2, out):
    N, D = x.shape
    DH = W2.shape[1]
    NB = N // P
    GB = 4
    GW = GB * P
    NG = N // GW
    PB = 2
    CHUNK = 512
    RING = 4
    PPC = CHUNK // (PB * P)
    K = RING * PPC
    BODY = K * PB
    IT = NB // BODY
    PG = NB // PB
    LOOK = 5
    PADW = LOOK * PB * P
    GC = 2 * DH + 1
    STEP_W = PB * GW
    NF = 4
    XL = 8

    adj_rows = adj.rearrange("(b p) n -> p b n", p=P)
    x_rows = x.rearrange("(b p) d -> p b d", p=P)
    out_rows = out.rearrange("(b p) d -> p b d", p=P)
    adj_diag = bass.AP(adj.tensor, 0, [[N + 1, P], [(N + 1) * P, NB]])

    ctx = ExitStack()
    with ctx:
        def sb(name, shape, dt):
            return ctx.enter_context(nc.sbuf_tensor(name, shape, dt))

        def pb(name, shape, dt):
            return ctx.enter_context(nc.psum_tensor(name, shape, dt))

        def sem(name):
            return ctx.enter_context(nc.semaphore(name))

        ctx.enter_context(nc.allow_non_contiguous_dma(reason="bias columns and the diagonal of adj"))

        res = sb("res", [P, NB, D], F32)
        hx_hi = sb("hx_hi", [P, N + PADW], F16)
        hx_lo = sb("hx_lo", [P, N + PADW], F16)
        g = sb("g", [P, NB, GC], F16)
        g_f = sb("g_f", [P, NB, DH + 1], F32)
        w_fix = sb("w_fix", [P, NB], F32)
        ring = sb("ring", [P, RING, GB, CHUNK], F32)
        ident_bf = sb("ident_bf", [P, P], BF16)
        ident_f = sb("ident_f", [P, P], F32)
        zeros = sb("zeros", [P, 2 * GC], F16)
        half = sb("half", [P, GB], F32)
        minus_one = sb("minus_one", [P, GB], F32)
        exp_bias = sb("exp_bias", [P, 1], F32)
        work = sb("work", [P, (2 + 2 * NF) * STEP_W], F32)
        xt = work[:, 0:N]
        tanh_b = [work[:, b * STEP_W:(b + 1) * STEP_W] for b in range(2)]
        f_b = [work[:, (2 + b) * STEP_W:(3 + b) * STEP_W] for b in range(NF)]
        p_b = [work[:, (2 + NF + b) * STEP_W:(3 + NF + b) * STEP_W] for b in range(NF)]
        wt = sb("wt", [P, D], F32)
        w12 = sb("w12", [P, 2 * DH], F32)
        b12 = sb("b12", [P, GB, 2 * DH], F32)
        cols = sb("cols", [P, 8], F32)
        gam, bet, btc, bts, bn_a, bn_b, one = (cols[:, i:i + 1] for i in range(7))
        stats = sb("stats", [P, NG, 6], F32)
        mv = sb("mv", [P, 2], F32)
        hx_f = sb("hx_f", [P, 2, GW], F32)
        hx_sq = sb("hx_sq", [P, 2, GW], F32)
        og = sb("og", [P, 2, GB, 2 * DH], F32)
        leak = sb("leak", [P, 2, GB, DH], F32)
        adj_ii = sb("adj_ii", [P, NB], F32)
        f_ii = sb("f_ii", [P, 2, NB], F32)
        sums = sb("sums", [P, GB, GC], F32)
        acc_s = sb("acc_s", [P, GB, DH + 1], F32)
        fix = sb("fix", [P, GB, DH + 1], F32)
        rden = sb("rden", [P, GB], F32)
        att = sb("att", [P, GB, DH], F32)
        att2 = sb("att2", [P, GB, DH], F32)
        cent = sb("cent", [P, GB, D], F32)
        sq = sb("sq", [P, GB, D], F32)
        mean = sb("mean", [P, GB], F32)
        var = sb("var", [P, GB], F32)

        scores = [pb(f"scores{i}", [P, STEP_W], F32) for i in range(2)]
        adj_t = [pb(f"adj_t{i}", [P, STEP_W], BF16) for i in range(2)]
        acc = [pb(f"acc{i}", [P, 512], F32) for i in range(2)]
        bank = [scores[i][:, j * 512:(j + 1) * 512] for i in range(2) for j in range(2)]
        s_ii = acc[0][:, 0:NB]

        par_loaded = sem("par_loaded")
        x_loaded = [sem(f"x_loaded{i}") for i in range(XL)]
        diag_loaded = sem("diag_loaded")
        const_made = sem("const_made")
        xt_ready, xt_copied, stats_made = sem("xt_ready"), sem("xt_copied"), sem("stats_made")
        bn_step, rstd_made = sem("bn_step"), sem("rstd_made")
        hn_even, hn_odd = sem("hn_even"), sem("hn_odd")
        hx_ready, hxf_made, hxsq_made, hi_made, lo_made = (sem("hx_ready"), sem("hxf_made"), sem("hxsq_made"),
                                                           sem("hi_made"), sem("lo_made"))
        og_ready, og_made, gfull_made, ghi_made, glo_made, leaky_made, out1_made = (
            sem("og_ready"), sem("og_made"), sem("gfull_made"), sem("ghi_made"), sem("glo_made"),
            sem("leaky_made"), sem("out1_made"))
        dots_done, fii_step, fix_step, pro_done = sem("dots_done"), sem("fii_step"), sem("fix_step"), sem("pro_done")
        adj_loaded = [sem(f"adj_loaded{i}") for i in range(RING)]
        scores_ready = sem("scores_ready")
        tanh_done = sem("tanh_done")
        exp_done = sem("exp_done")
        split_done = sem("split_done")
        adjt_ready = sem("adjt_ready")
        masked = sem("masked")
        f_free = sem("f_free")
        p_free = sem("p_free")
        sums_copied = sem("sums_copied")
        epi_step = sem("epi_step")
        epi_turn = sem("epi_turn")
        stored = sem("stored")
        last_step, last_rstd = sem("last_step"), sem("last_rstd")
        stored_last = sem("stored_last")

        START = 1

        block = ctx.enter_context(nc.Block())
        HALVINGS = int(math.log2(D))
        EPI = 15 + 2 * HALVINGS
        LAST_STEPS = 17

        PARAMS = 6 + 2 * GB

        @block.sync
        def _(sp):
            XQ = NB // XL
            for i in range(XL):
                sp.dma_start(res[:, i * XQ:(i + 1) * XQ, :], x_rows[:, i * XQ:(i + 1) * XQ, :]).then_inc(x_loaded[i], 16)
            col = lambda v: v.rearrange("(p o) -> p o", o=1)
            row = lambda v: v.rearrange("(o n) -> o n", o=1).to_broadcast([P, DH])
            for dst, src in ((gam, col(gamma)), (bet, col(beta)), (btc, col(bt)), (wt[:, :], Wt),
                             (w12[:, 0:DH], W1), (w12[:, DH:2 * DH], W2)):
                sp.dma_start(dst, src).then_inc(par_loaded, 16)
            for r in range(GB):
                sp.dma_start(b12[:, r, 0:DH], row(b1)).then_inc(par_loaded, 16)
                sp.dma_start(b12[:, r, DH:2 * DH], row(b2)).then_inc(par_loaded, 16)
            for c in range(RING):
                sp.dma_start(ring[:, c, :, :], adj_rows[:, 0:GB, c * CHUNK:(c + 1) * CHUNK]).then_inc(adj_loaded[c], 16)
            sp.dma_start(adj_ii[:, :], adj_diag).then_inc(diag_loaded, 16)
            with sp.Fori(1, IT) as it:
                for c in range(RING):
                    sp.wait_ge(adjt_ready, (it - 1) * K + (c + 1) * PPC)
                    sp.dma_start(ring[:, c, :, :],
                                 adj_rows[:, 0:GB, bass.ds(it * (RING * CHUNK) + c * CHUNK, CHUNK)]
                                 ).then_inc(adj_loaded[c], 16)
            with sp.Fori(1, NG) as s:
                with sp.Fori(0, IT) as it:
                    for c in range(RING):
                        sp.wait_ge(adjt_ready, (s * IT + it - 1) * K + (c + 1) * PPC)
                        sp.dma_start(ring[:, c, :, :],
                                     adj_rows[:, bass.ds(s * GB, GB), bass.ds(it * (RING * CHUNK) + c * CHUNK, CHUNK)]
                                     ).then_inc(adj_loaded[c], 16)
            sp.wait_ge(last_step, LAST_STEPS + GB)
            sp.dma_start(out_rows[:, NB - GB:NB, :], res[:, NB - GB:NB, :]).then_inc(stored_last, 16)
            sp.wait_ge(stored_last, 16)

        @block.gpsimd
        def _(pool):
            pool.sem_inc(epi_step, START)
            nc.gpsimd.memset(ident_f[:, :], 0.0).then_inc(const_made, 1)
            nc.gpsimd.memset(ident_bf[:, :], 0.0).then_inc(const_made, 1)
            pool.wait_ge(const_made, 2)
            for m in (ident_f, ident_bf):
                nc.gpsimd.affine_select(out=m[:, :], in_=m[:, :], compare_op=ALU.not_equal, fill=1.0,
                                        base=0, pattern=[[-1, P]], channel_multiplier=1).then_inc(const_made, 1)
            nc.gpsimd.memset(zeros[:, :], 0.0).then_inc(const_made, 1)
            nc.gpsimd.memset(one, 1.0).then_inc(const_made, 1)
            nc.gpsimd.memset(half[:, :], -0.5).then_inc(const_made, 1)
            nc.gpsimd.memset(exp_bias[:, :], math.log(PS) - 0.5).then_inc(const_made, 1)
            nc.gpsimd.memset(g[:, :, DH:DH + 1], GS).then_inc(const_made, 1)
            nc.gpsimd.memset(g_f[:, :, DH:DH + 1], GS).then_inc(const_made, 1)
            nc.gpsimd.memset(minus_one[:, :], -1.0).then_inc(const_made, 1)
            pool.wait_ge(const_made, 11)
            pool.wait_ge(bn_step, 2)
            nc.gpsimd.tensor_tensor(bn_a, mv[:, 1:2], half[:, 0:1], ALU.pow).then_inc(rstd_made, 1)
            for i in range(NG):
                pool.wait_ge(leaky_made, i + 1)
                dst = res[:, i * GB:(i + 1) * GB, 0:DH]
                nc.gpsimd.tensor_tensor(dst, dst, leak[:, i % 2, :, :], ALU.add).then_inc(out1_made, 1)
            pool.wait_ge(out1_made, NG)
            def bc(v, w):
                return v.rearrange("p (b o) -> p b o", o=1).to_broadcast([P, GB, w])

            def row_sums(src, dst):
                w = D // 2
                while w:
                    yield nc.gpsimd.tensor_tensor(dst[:, :, 0:w], src[:, :, 0:w], src[:, :, w:2 * w], ALU.add)
                    src, w = dst, w // 2

            def epilogue(rows, fixed, w):
                tt, ts = nc.gpsimd.tensor_tensor, nc.gpsimd.tensor_scalar
                lower = rows[:, :, DH:D]
                yield tt(fix[:, :, :], fixed, bc(w, DH + 1), ALU.mult)
                yield tt(acc_s[:, :, :], sums[:, :, 0:DH + 1], fix[:, :, :], ALU.add)
                yield tt(acc_s[:, :, 0:DH], acc_s[:, :, 0:DH], sums[:, :, DH + 1:GC], ALU.add)
                yield tt(rden[:, :], acc_s[:, :, DH], minus_one[:, :], ALU.pow)
                yield tt(att[:, :, :], acc_s[:, :, 0:DH], bc(rden[:, :], DH), ALU.mult)
                yield ts(att2[:, :, :], att[:, :, :], 0.0, LEAKY, ALU.min, ALU.mult)
                yield ts(att[:, :, :], att[:, :, :], 0.0, None, ALU.max)
                yield tt(att[:, :, :], att[:, :, :], att2[:, :, :], ALU.add)
                yield tt(lower, lower, att[:, :, :], ALU.add)
                yield from row_sums(rows, cent)
                yield ts(mean[:, :], cent[:, :, 0], 1.0 / D, None, ALU.mult)
                yield tt(cent[:, :, :], rows, bc(mean[:, :], D), ALU.subtract)
                yield tt(sq[:, :, :], cent[:, :, :], cent[:, :, :], ALU.mult)
                yield from row_sums(sq, sq)
                yield ts(var[:, :], sq[:, :, 0], 1.0 / D, LN_EPS, ALU.mult, ALU.add)
                yield tt(var[:, :], var[:, :], half[:, :], ALU.pow)
                yield tt(rows, cent[:, :, :], bc(var[:, :], D), ALU.mult)

            with pool.Fori(1, NG) as s:
                rows = res[:, bass.ds(s * GB - GB, GB), :]
                steps = epilogue(rows, g_f[:, bass.ds(s * GB - GB, GB), :], w_fix[:, bass.ds(s * GB - GB, GB)])
                for e in range(EPI):
                    if e == 0:
                        pool.wait_ge(sums_copied, 2 * s + START)
                    else:
                        pool.wait_ge(epi_step, (s - 1) * EPI + e + START)
                    pool.sem_inc(epi_turn, 1)
                    next(steps).then_inc(epi_step, 1)
                pool.wait_ge(epi_step, s * EPI + START)
                pool.sem_inc(epi_turn, 1)
                pool.dma_start(out_rows[:, bass.ds(s * GB - GB, GB), :], rows).then_inc(stored, 16)
            pool.wait_ge(last_step, LAST_STEPS)
            nc.gpsimd.tensor_tensor(var[:, :], var[:, :], half[:, :], ALU.pow).then_inc(last_rstd, 1)
            pool.wait_ge(stored, 16 * (NG - 1))

        @block.scalar
        def _(act):
            act.sem_inc(exp_done, START)
            act.sem_inc(sums_copied, START)
            for i in range(NG):
                act.wait_ge(xt_ready, i + 1)
                nc.scalar.copy(xt[:, i * GW:(i + 1) * GW], bank[i % 4]).then_inc(xt_copied, 1)
            act.wait_ge(bn_step, 6)

            def normalise(i):
                c = xt[:, i * GW:(i + 1) * GW]
                nc.scalar.activation(c, c, ACT.Identity, bias=bn_b, scale=bn_a).then_inc(hn_odd, 1)

            normalise(1)

            def scale_g(i):
                act.wait_ge(og_made, i + 1)
                blocks = slice(i * GB, (i + 1) * GB)
                g_in = og[:, i % 2, :, DH:2 * DH]
                nc.scalar.mul(g_f[:, blocks, 0:DH], g_in, GS).then_inc(gfull_made, 1)
                nc.scalar.mul(g[:, blocks, 0:DH], g_in, GS).then_inc(ghi_made, 1)

            for i in range(NG):
                act.wait_ge(hx_ready, i + 1)
                if i >= 2:
                    act.wait_ge(lo_made, i - 1)
                nc.scalar.activation(hx_f[:, i % 2, :], bank[i % 2], ACT.Identity, bias=bts, scale=HS).then_inc(hxf_made, 1)
                act.wait_ge(hxf_made, i + 1)
                if i >= 2:
                    act.wait_ge(dots_done, i - 1)
                nc.scalar.activation(hx_sq[:, i % 2, :], hx_f[:, i % 2, :], ACT.Square, scale=1.0 / HS).then_inc(hxsq_made, 1)
                if i % 2 and i + 2 < NG:
                    normalise(i + 2)
                if i:
                    scale_g(i - 1)
            scale_g(NG - 1)
            act.wait_ge(dots_done, NG)
            nc.scalar.activation(f_ii[:, 0, :], s_ii, ACT.Tanh, scale=0.5).then_inc(fii_step, 1)
            act.wait_ge(fii_step, 1)
            nc.scalar.activation(f_ii[:, 1, :], f_ii[:, 0, :], ACT.Exp, scale=0.5, bias=exp_bias[:, :]).then_inc(fii_step, 1)

            def tanh(q, b):
                act.wait_ge(scores_ready, q + 1)
                nc.scalar.activation(tanh_b[b], scores[b][:, :], ACT.Tanh, scale=0.5 / (HS * HS)).then_inc(tanh_done, 1)

            def expo(q, k):
                act.wait_ge(tanh_done, q + 1)
                act.wait_ge(f_free, q + 1)
                nc.scalar.activation(f_b[k % NF], tanh_b[k % 2], ACT.Exp, scale=0.5, bias=exp_bias[:, :]).then_inc(exp_done, 1)

            def body(n, done=None, last=False):
                for k in range(K):
                    if done is not None and k == LOOK - 2:
                        copy_sums(done)
                    if not (last and k == K - 1):
                        act.wait_ge(exp_done, n * K + k + START)
                        tanh(n * K + k + 1, (k + 1) % 2)
                    expo(n * K + k, k)

            def copy_sums(s):
                act.wait_ge(p_free, s * PG + NF)
                act.wait_ge(epi_step, (s - 1) * EPI + START)
                for h in range(2):
                    nc.scalar.copy(sums[:, 2 * h:2 * h + 2, :].rearrange("p b n -> p (b n)"),
                                   acc[h][:, 0:2 * GC]).then_inc(sums_copied, 1)

            tanh(0, 0)
            with act.Fori(0, IT) as it:
                body(it)
            with act.Fori(1, NG - 1) as s:
                body(s * IT, done=s)
                with act.Fori(1, IT) as it:
                    body(s * IT + it)
            body((NG - 1) * IT, done=NG - 1)
            with act.Fori(1, IT - 1) as it:
                body((NG - 1) * IT + it)
            body(NG * IT - 1, last=True)
            copy_sums(NG)

        @block.vector
        def _(dve):
            dve.sem_inc(f_free, NF)
            for i in range(NG):
                dve.wait_ge(xt_copied, i + 1)
                nc.vector.bn_stats(stats[:, i, :], xt[:, i * GW:(i + 1) * GW]).then_inc(stats_made, 1)
            dve.wait_ge(stats_made, NG)
            nc.vector.bn_aggr(mv[:, :], stats[:, :, :]).then_inc(bn_step, 1)
            dve.wait_ge(bn_step, 1)
            nc.vector.tensor_scalar(mv[:, 1:2], mv[:, 1:2], BN_EPS, None, ALU.add).then_inc(bn_step, 1)
            dve.wait_ge(rstd_made, 1)
            dve.wait_ge(par_loaded, 16 * PARAMS)
            nc.vector.tensor_tensor(bn_a, bn_a, gam, ALU.mult).then_inc(bn_step, 1)
            dve.wait_ge(bn_step, 3)
            nc.vector.tensor_scalar(mv[:, 1:2], bn_a, -1.0, None, ALU.mult).then_inc(bn_step, 1)
            nc.vector.tensor_scalar(bts, btc, HS, None, ALU.mult).then_inc(bn_step, 1)
            dve.wait_ge(bn_step, 5)
            nc.vector.scalar_tensor_tensor(out=bn_b, in0=mv[:, 0:1], scalar=mv[:, 1:2], in1=bet,
                                           op0=ALU.mult, op1=ALU.add).then_inc(bn_step, 1)
            dve.wait_ge(bn_step, 6)

            def normalise(i):
                c = xt[:, i * GW:(i + 1) * GW]
                nc.vector.tensor_scalar(c, c, bn_a, bn_b, ALU.mult, ALU.add).then_inc(hn_even, 1)

            normalise(0)

            def low_of_g(i):
                dve.wait_ge(gfull_made, i + 1)
                dve.wait_ge(ghi_made, i + 1)
                b = slice(i * GB, (i + 1) * GB)
                nc.vector.tensor_tensor(g[:, b, DH + 1:GC], g_f[:, b, 0:DH], g[:, b, 0:DH],
                                        ALU.subtract).then_inc(glo_made, 1)

            dve.wait_ge(const_made, 11)
            for i in range(NG):
                if i % 2 == 0 and i + 2 < NG:
                    normalise(i + 2)
                c = slice(i * GW, (i + 1) * GW)
                dve.wait_ge(hxf_made, i + 1)
                nc.vector.tensor_copy(hx_hi[:, c], hx_f[:, i % 2, :]).then_inc(hi_made, 1)
                dve.wait_ge(og_ready, i + 1)
                if i >= 2:
                    dve.wait_ge(ghi_made, i - 1)
                    dve.wait_ge(leaky_made, i - 1)
                nc.vector.tensor_tensor(og[:, i % 2, :, :], bank[2 + i % 2].rearrange("p (b n) -> p b n", b=GB),
                                        b12[:, :, :], ALU.add).then_inc(og_made, 1)
                dve.wait_ge(hi_made, i + 1)
                nc.vector.tensor_tensor(hx_lo[:, c], hx_f[:, i % 2, :], hx_hi[:, c], ALU.subtract).then_inc(lo_made, 1)
                dve.wait_ge(og_made, i + 1)
                if i >= 2:
                    dve.wait_ge(out1_made, i - 1)
                h1 = og[:, i % 2, :, 0:DH]
                nc.vector.scalar_tensor_tensor(out=leak[:, i % 2, :, :], in0=h1, scalar=LEAKY, in1=h1,
                                               op0=ALU.mult, op1=ALU.max).then_inc(leaky_made, 1)
                if i >= 2:
                    low_of_g(i - 2)
            low_of_g(NG - 2)
            low_of_g(NG - 1)
            dve.wait_ge(hi_made, NG)
            dve.wait_ge(lo_made, NG)
            nc.vector.tensor_copy(hx_hi[:, N:N + PADW], hx_hi[:, 0:PADW]).then_inc(hi_made, 1)
            nc.vector.tensor_copy(hx_lo[:, N:N + PADW], hx_lo[:, 0:PADW]).then_inc(lo_made, 1)
            dve.wait_ge(fii_step, 2)
            dve.wait_ge(diag_loaded, 16)
            nc.vector.scalar_tensor_tensor(out=f_ii[:, 0, :], in0=adj_ii[:, :], scalar=0.0, in1=f_ii[:, 1, :],
                                           op0=ALU.is_gt, op1=ALU.mult).then_inc(fix_step, 1)
            dve.wait_ge(fix_step, 1)
            nc.vector.tensor_scalar(w_fix[:, :], f_ii[:, 0, :], -1.0, PS, ALU.mult, ALU.add).then_inc(fix_step, 1)

            def split(q, k):
                dve.wait_ge(exp_done, q + 1 + START)
                f = f_b[k % NF]
                nc.vector.tensor_tensor(f.bitcast(F16)[:, 0::2], f, f.bitcast(BF16)[:, 1::2],
                                        ALU.subtract).then_inc(split_done, 1)

            def mask(q, k):
                dve.wait_ge(split_done, q + 1)
                dve.wait_ge(adjt_ready, q + 1)
                dve.wait_ge(p_free, q + 1)
                nc.vector.scalar_tensor_tensor(out=p_b[k % NF], in0=adj_t[k % 2][:, :], scalar=0.0, in1=f_b[k % NF],
                                               op0=ALU.is_gt, op1=ALU.mult).then_inc(f_free, 1)

            split(0, 0)
            with dve.Fori(0, NG * IT - 1) as n:
                for k in range(K):
                    split(n * K + k + 1, k + 1)
                    mask(n * K + k, k)
            for k in range(K):
                if k + 1 < K:
                    split((NG * IT - 1) * K + k + 1, k + 1)
                mask((NG * IT - 1) * K + k, k)

            n = [0]

            def then(ins):
                n[0] += 1
                ins.then_inc(last_step, 1)

            def bc(v, w):
                return v.rearrange("p (b o) -> p b o", o=1).to_broadcast([P, GB, w])

            rows = res[:, NB - GB:NB, :]
            lower = rows[:, :, DH:D]
            dve.wait_ge(sums_copied, 2 * NG + START)
            dve.wait_ge(epi_step, EPI * (NG - 1) + START)
            then(nc.vector.tensor_tensor(fix[:, :, :], g_f[:, NB - GB:NB, :], bc(w_fix[:, NB - GB:NB], DH + 1), ALU.mult))
            dve.wait_ge(last_step, n[0])
            then(nc.vector.tensor_tensor(acc_s[:, :, :], sums[:, :, 0:DH + 1], fix[:, :, :], ALU.add))
            dve.wait_ge(last_step, n[0])
            then(nc.vector.tensor_tensor(acc_s[:, :, 0:DH], acc_s[:, :, 0:DH], sums[:, :, DH + 1:GC], ALU.add))
            then(nc.vector.reciprocal(rden[:, :].rearrange("p (b o) -> p b o", o=1), acc_s[:, :, DH:DH + 1]))
            dve.wait_ge(last_step, n[0])
            then(nc.vector.tensor_tensor(att[:, :, :], acc_s[:, :, 0:DH], bc(rden[:, :], DH), ALU.mult))
            dve.wait_ge(last_step, n[0])
            then(nc.vector.scalar_tensor_tensor(out=att2[:, :, :], in0=att[:, :, :], scalar=LEAKY, in1=att[:, :, :],
                                                op0=ALU.mult, op1=ALU.max))
            dve.wait_ge(last_step, n[0])
            then(nc.vector.tensor_tensor(lower, lower, att2[:, :, :], ALU.add))
            dve.wait_ge(last_step, n[0])
            for b in range(GB):
                then(nc.vector.bn_stats(stats[:, b, :], rows[:, b, :]))
            dve.wait_ge(last_step, n[0])
            for b in range(GB):
                then(nc.vector.bn_aggr(stats[:, GB + b, 0:2], stats[:, b, :]))
            dve.wait_ge(last_step, n[0])
            then(nc.vector.tensor_scalar(var[:, :].rearrange("p (b o) -> p b o", o=1), stats[:, GB:2 * GB, 1:2],
                                         LN_EPS, None, ALU.add))
            then(nc.vector.tensor_copy(mean[:, :].rearrange("p (b o) -> p b o", o=1), stats[:, GB:2 * GB, 0:1]))
            assert n[0] == LAST_STEPS
            dve.wait_ge(last_step, n[0])
            dve.wait_ge(last_rstd, 1)
            for b in range(GB):
                then(nc.vector.tensor_scalar(rows[:, b, :], rows[:, b, :], mean[:, b:b + 1], var[:, b:b + 1],
                                             ALU.subtract, ALU.mult))

        @block.tensor
        def _(pe):
            pe.sem_inc(p_free, NF)
            pe.wait_ge(const_made, 10)
            for i in range(NG):
                if i % (NG // XL) == 0:
                    pe.wait_ge(x_loaded[i // (NG // XL)], 16)
                if i >= 4:
                    pe.wait_ge(xt_copied, i - 3)
                for b in range(GB):
                    t = nc.tensor.transpose(bank[i % 4][:, b * P:(b + 1) * P], res[:, i * GB + b, :], ident_f[:, :])
                t.then_inc(xt_ready, 1)
            pe.wait_ge(par_loaded, 16 * PARAMS)
            pe.wait_ge(xt_copied, NG)
            for i in range(NG + 1):
                if i < NG:
                    pe.wait_ge((hn_even, hn_odd)[i % 2], i // 2 + 1)
                    if i >= 2:
                        pe.wait_ge(hxf_made, i - 1)
                    c = xt[:, i * GW:(i + 1) * GW]
                    nc.tensor.matmul(bank[i % 2], wt[:, :], c, start=True, stop=True).then_inc(hx_ready, 1)
                    if i >= 2:
                        pe.wait_ge(og_made, i - 1)
                    for b in range(GB):
                        m = nc.tensor.matmul(bank[2 + i % 2][:, b * P:(b + 1) * P], c[:, b * P:(b + 1) * P], w12[:, :],
                                             start=True, stop=True)
                    m.then_inc(og_ready, 1)
                if i:
                    pe.wait_ge(hxsq_made, i)
                    for b in range(GB):
                        blk = (i - 1) * GB + b
                        m = nc.tensor.matmul(s_ii[:, blk:blk + 1], hx_sq[:, (i - 1) % 2, b * P:(b + 1) * P], one,
                                             start=True, stop=True)
                    m.then_inc(dots_done, 1)

            def make_scores(q, k, jcol, icol, fresh=False):
                if not fresh:
                    pe.wait_ge(tanh_done, q - 1)
                for t in range(PB):
                    o = scores[k % 2][:, t * GW:(t + 1) * GW]
                    j = bass.ds(jcol + t * P, P)
                    i = bass.ds(icol, GW)
                    nc.tensor.matmul(o, hx_hi[:, j], hx_hi[:, i], start=True, stop=False)
                    nc.tensor.matmul(o, hx_hi[:, j], hx_lo[:, i], start=False, stop=False)
                    m = nc.tensor.matmul(o, hx_lo[:, j], hx_hi[:, i], start=False, stop=True)
                m.then_inc(scores_ready, 1)

            def transpose_adj(q, k, loads):
                c = (k // PPC) % RING
                pe.wait_ge(adj_loaded[c], 16 * loads)
                if q is not None:
                    pe.wait_ge(f_free, q - 1 + NF)
                upper = ring[:, c, :, :].bitcast(BF16)[:, :, 1::2]
                for t in range(PB):
                    for b in range(GB):
                        o = (t * GB + b) * P
                        col = ((k % PPC) * PB + t) * P
                        m = nc.tensor.transpose(adj_t[k % 2][:, o:o + P], upper[:, b, col:col + P], ident_bf[:, :])
                        if t == PB - 1 and b == GB - 1:
                            m.then_inc(adjt_ready, 1)
                return m

            def product(q, k, blk):
                pe.wait_ge(f_free, q + 1 + NF)
                p_hi = p_b[k % NF].bitcast(BF16)[:, 1::2]
                p_lo = p_b[k % NF].bitcast(F16)[:, 0::2]
                for part, width in ((p_hi, GC), (p_lo, DH + 1)):
                    for t in range(PB):
                        for b in range(GB):
                            o = (t * GB + b) * P
                            col = (b % 2) * GC
                            m = nc.tensor.matmul(acc[b // 2][:, col:col + width], part[:, o:o + P],
                                                 g[:, bass.ds(blk + t, 1), 0:width],
                                                 start=False, stop=part is p_lo, skip_group_check=True)
                m.then_inc(p_free, 1)

            pe.wait_ge(hxf_made, NG)
            pe.wait_ge(og_made, NG)
            pe.wait_ge(hi_made, NG)
            pe.wait_ge(lo_made, NG)
            for k in range(LOOK):
                make_scores(k, k, k * PB * P, 0, fresh=k < 2)
            transpose_adj(None, 0, 1)
            pe.wait_ge(hi_made, NG + 1)
            pe.wait_ge(lo_made, NG + 1)
            pe.wait_ge(glo_made, NG)
            pe.wait_ge(fii_step, 1)

            def clear_sums(s):
                pe.wait_ge(sums_copied, s * 2 + START)
                for h in range(2):
                    nc.tensor.matmul(acc[h][:, 0:2 * GC], zeros[:, 0:P], zeros[:, :], start=True, stop=False,
                                     skip_group_check=True)

            def body(n, it, last=False):
                for k in range(K):
                    q = n * K + k
                    nk, lk = k + 1, k + LOOK
                    if not (last and nk == K):
                        transpose_adj(q + 1, nk % K, n + 1 + nk // K)
                    product(q, k, it * BODY + k * PB)
                    if not (last and lk >= K):
                        make_scores(q + LOOK, lk, it * (BODY * P) + lk * PB * P, ((n + lk // K) // IT) * GW)

            with pe.Fori(0, NG - 1) as s:
                clear_sums(s)
                with pe.Fori(0, IT) as it:
                    body(s * IT + it, it)
            clear_sums(NG - 1)
            with pe.Fori(0, IT - 1) as it:
                body((NG - 1) * IT + it, it)
            body(NG * IT - 1, IT - 1, last=True)


_INS = ['x', 'adj', 'L0_gnn_gamma', 'L0_gnn_beta', 'L0_gnn_Wt', 'L0_gnn_bt', 'L0_gnn_W1', 'L0_gnn_b1',
        'L0_gnn_W2', 'L0_gnn_b2']


def kernel(**inputs):
    import numpy as _np
    import concourse.bacc as _bacc
    from concourse import mybir as _mybir
    from concourse.bass_utils import run_bass_kernel_spmd as _run

    nc = _bacc.Bacc("TRN2", target_bir_lowering=False, num_devices=1)
    arrays, args = {}, []
    for name in _INS:
        a = _np.ascontiguousarray(inputs[name])
        arrays[f"in_{name}_dram"] = a
        args.append(nc.dram_tensor(f"in_{name}_dram", a.shape, _mybir.dt.from_np(a.dtype), kind="ExternalInput").ap())
    out = nc.dram_tensor("out_0_dram", inputs['x'].shape, _mybir.dt.float32, kind="ExternalOutput").ap()
    gnn_kernel(nc, *args, out)
    r = _run(nc, [arrays], core_ids=[0])
    return r.results[0]["out_0_dram"]
```
